# Optimizing a Trainium2 kernel written in Bass

```python
import numpy as np
import jax
import jax.numpy as jnp

def _softmax(x, axis=-1):
    return jax.nn.softmax(x, axis=axis)
def _gelu(x):
    return jax.nn.gelu(x, approximate=True)
def _silu(x):
    return jax.nn.silu(x)
def _sigmoid(x):
    return jax.nn.sigmoid(x)
def _layernorm(x, axis=-1, eps=1e-5):
    m = jnp.mean(x, axis=axis, keepdims=True)
    v = jnp.var(x, axis=axis, keepdims=True)
    return (x - m) / jnp.sqrt(v + eps)
def _scatter_add(tgt, idx, src, axis=0):
    return tgt.at[idx].add(src)
def _segment_sum(src, seg, n):
    return jax.ops.segment_sum(src, seg, n)

kernel_name = 'mk_conv_preact_d1_conv_nchw512_e91004'

def setup_inputs(seed: int = 0):
    np.random.seed(seed)
    _w = jnp.asarray
    def _rec_inputs():
        import jax
        import jax.numpy as jnp
        _gk = jax.random.key(seed)
        x = -7.109e-05 + 0.9999 * jax.random.normal(jax.random.fold_in(_gk, 1), (2, 512, 256, 256), jnp.float32)
        return x
    x = _rec_inputs()
    def _L0_conv_setup():
        import jax, jax.numpy as jnp
        import numpy as np
        B, C, H, W = (2, 512, 256, 256)
        EPS = 1e-05

        def _dwconv(x, k):
            return jax.lax.conv_general_dilated(x, k, window_strides=(1, 1), padding='VALID', dimension_numbers=('NCHW', 'OIHW', 'NCHW'), feature_group_count=x.shape[1])

        def _bn_relu(y, gamma, beta):
            m = jnp.mean(y, axis=(0, 2, 3), keepdims=True)
            v = jnp.var(y, axis=(0, 2, 3), keepdims=True)
            yn = (y - m) * jax.lax.rsqrt(v + EPS)
            return jax.nn.relu(yn * gamma.reshape(1, -1, 1, 1) + beta.reshape(1, -1, 1, 1))
        key = jax.random.key(seed)
        ks = jax.random.split(key, 11)
        inp = {'x': jax.random.normal(ks[0], (B, C, H, W), dtype=jnp.float32), 'w1': jax.random.normal(ks[1], (C, 1, H, 1), dtype=jnp.float32) * 0.05, 'w2': jax.random.normal(ks[2], (C, 1, 1, W), dtype=jnp.float32) * 0.05, 'g1': jax.random.uniform(ks[3], (C,), dtype=jnp.float32) + 0.5, 'b1': jax.random.normal(ks[4], (C,), dtype=jnp.float32) * 0.1, 'g2': jax.random.uniform(ks[5], (C,), dtype=jnp.float32) + 0.5, 'b2': jax.random.normal(ks[6], (C,), dtype=jnp.float32) * 0.1, 'lw1': jax.random.normal(ks[7], (2 * C, C), dtype=jnp.float32) * 0.02, 'lb1': jax.random.normal(ks[8], (2 * C,), dtype=jnp.float32) * 0.02, 'lw2': jax.random.normal(ks[9], (C, 2 * C), dtype=jnp.float32) * 0.02, 'lb2': jax.random.normal(ks[10], (C,), dtype=jnp.float32) * 0.02}
        return inp
    _L0_conv_all = _L0_conv_setup()
    _L0_conv_in = {k: v for k, v in _L0_conv_all.items() if k in ('w1', 'w2', 'g1', 'b1', 'g2', 'b2', 'lw1', 'lb1', 'lw2', 'lb2', )}
    del _L0_conv_all

    return {
        "x": x,
        "L0_conv_w1": _L0_conv_in["w1"],
        "L0_conv_w2": _L0_conv_in["w2"],
        "L0_conv_g1": _L0_conv_in["g1"],
        "L0_conv_b1": _L0_conv_in["b1"],
        "L0_conv_g2": _L0_conv_in["g2"],
        "L0_conv_b2": _L0_conv_in["b2"],
        "L0_conv_lw1": _L0_conv_in["lw1"],
        "L0_conv_lb1": _L0_conv_in["lb1"],
        "L0_conv_lw2": _L0_conv_in["lw2"],
        "L0_conv_lb2": _L0_conv_in["lb2"],
    }

def reference(x, L0_conv_w1, L0_conv_w2, L0_conv_g1, L0_conv_b1, L0_conv_g2, L0_conv_b2, L0_conv_lw1, L0_conv_lb1, L0_conv_lw2, L0_conv_lb2):
    import jax
    import jax.numpy as jnp
    def _L0_conv_ref(x, w1, w2, g1, b1, g2, b2, lw1, lb1, lw2, lb2):
        import jax, jax.numpy as jnp
        import numpy as np
        B, C, H, W = (2, 512, 256, 256)
        EPS = 1e-05

        def _dwconv(x, k):
            return jax.lax.conv_general_dilated(x, k, window_strides=(1, 1), padding='VALID', dimension_numbers=('NCHW', 'OIHW', 'NCHW'), feature_group_count=x.shape[1])

        def _bn_relu(y, gamma, beta):
            m = jnp.mean(y, axis=(0, 2, 3), keepdims=True)
            v = jnp.var(y, axis=(0, 2, 3), keepdims=True)
            yn = (y - m) * jax.lax.rsqrt(v + EPS)
            return jax.nn.relu(yn * gamma.reshape(1, -1, 1, 1) + beta.reshape(1, -1, 1, 1))
        b, c, h, w = x.shape
        xl1 = _bn_relu(_dwconv(x, w1), g1, b1)
        xl2 = _bn_relu(_dwconv(x, w2), g2, b2)
        dot_cb = jnp.einsum('bck,bck->cb', xl1[:, :, 0, :], xl2[:, :, :, 0])
        num = dot_cb.reshape(b, c)
        num = num @ lw1.T + lb1
        num = num @ lw2.T + lb2
        num = jax.nn.softmax(num, axis=1)
        return x * num[:, :, None, None]

    def _gn(v, G=32, eps=1e-5):
        B_, C_, H_, W_ = v.shape
        g = v.reshape(B_, G, C_ // G, H_, W_)
        m = jnp.mean(g, axis=(2, 3, 4), keepdims=True)
        s = jnp.var(g, axis=(2, 3, 4), keepdims=True)
        return ((g - m) / jnp.sqrt(s + eps)).reshape(v.shape)

    def _ln_c(v, eps=1e-6):
        m = jnp.mean(v, axis=1, keepdims=True)
        s = jnp.var(v, axis=1, keepdims=True)
        return (v - m) / jnp.sqrt(s + eps)

    def _ln_t(v, eps=1e-5):
        m = jnp.mean(v, axis=-1, keepdims=True)
        s = jnp.var(v, axis=-1, keepdims=True)
        return (v - m) / jnp.sqrt(s + eps)

    def _to_tokens(v):
        B_, C_, H_, W_ = v.shape
        return v.reshape(B_, C_, H_ * W_).transpose(0, 2, 1)
    def _from_tokens(t, like):
        B_, C_, H_, W_ = like.shape
        return t.transpose(0, 2, 1).reshape(B_, C_, H_, W_)

    x = x + _L0_conv_ref(_gn(x), L0_conv_w1, L0_conv_w2, L0_conv_g1, L0_conv_b1, L0_conv_g2, L0_conv_b2, L0_conv_lw1, L0_conv_lb1, L0_conv_lw2, L0_conv_lb2)
    return x


_drawn_inputs = setup_inputs


def setup_inputs(seed=0):
    import zlib

    import numpy as np

    out = dict(_drawn_inputs(seed))
    spreads = {}
    factors = {'L0_conv_w1': 3.719,
     'L0_conv_w2': 181.262,
     'L0_conv_g1': 8.0,
     'L0_conv_b1': 17.115,
     'L0_conv_b2': 8.0,
     'L0_conv_lb1': 200.0,
     'L0_conv_lb2': 200.0,
     'L0_conv_g2': 8.0}
    for name, (base, spread) in spreads.items():
        noise = np.random.default_rng([zlib.crc32(name.encode()), seed]).standard_normal(out[name].shape)
        drawn = base * np.exp(spread * noise) if base else spread * noise
        out[name] = jnp.asarray(drawn.astype(out[name].dtype))
    for name, factor in factors.items():
        out[name] = (out[name] * factor).astype(out[name].dtype)
    return out
```

```python
import concourse.bass as bass
from concourse import mybir
from contextlib import ExitStack

P = 128
B, C, H, W = 2, 512, 256, 256
G = 32
CG = C // G
E = P // CG
JR = H // E
JH = JR // 2
S = 4
UNITS = 2 * G
ROUNDS = UNITS // S
GB = 8
BLOCKS = G // GB
BANK_GROUPS = 4
PAIRS = B * JH // 2
HID = 2 * C
HT = HID // P
CT = C // P
GROUP_N = CG * H * W
BN_N = B * W
EPS = 1e-5


def conv_preact(nc, x, w1, w2, g1, b1, g2, b2, w2_rows, lw1, lb1, lw2, lb2, out):
    f32 = mybir.dt.float32
    bf16 = mybir.dt.bfloat16
    ALU = mybir.AluOpType
    ACT = mybir.ActivationFunctionType
    AX = mybir.AxisListType

    x_v = x.rearrange("b (g c) (e j) w -> g (c e) b (j w)", c=CG, e=E)
    out_v = out.rearrange("b (g c) (e j) w -> g (c e) b (j w)", c=CG, e=E)
    w2_v = w2_rows.rearrange("(g c) w -> g c w", c=CG)
    HALF = JH * W

    with ExitStack() as ctx:
        def sb(name, shape, dt=f32):
            return ctx.enter_context(nc.sbuf_tensor(name, shape, dt))

        def pb(name, shape):
            return ctx.enter_context(nc.psum_tensor(name, shape, f32))

        def sem(name):
            return ctx.enter_context(nc.semaphore(name))

        xs = sb("xs", [P, S, B, HALF])
        lw2_sb = sb("lw2_sb", [P, HT, C])
        arena = lw2_sb[:].rearrange("p o c -> p (o c)")
        taps = arena[:, 0:2048].rearrange("p (i j m) -> p i j m", i=2, m=2 * CG)
        w1_sb = arena[:, 2048:3072].rearrange("p (g j) -> p g j", g=G)
        w2_row = arena[:, 3072:3584].rearrange("p (i w) -> p i w", i=2)
        y_sb = arena[:, 3584:4096].rearrange("p (b w) -> p b w", b=B)
        w2_sb = sb("w2_sb", [P, G, JR])
        own = sb("own", [P, CG])
        same = sb("same", [P, P])
        fold = sb("fold", [P, 15 * CG])
        spread = sb("spread", [P, GB, P])
        quad_ones = sb("quad_ones", [P, 4, P])
        all_ones = sb("all_ones", [P, P])
        eye2 = sb("eye2", [B, B])
        y = [sb("y1", [P, G, B, JR]), sb("y2", [P, G, B, JR])]
        y1, y2 = y
        y_sum = sb("y_sum", [P, 2 * BLOCKS, B])
        sq_sum = sb("sq_sum", [P, G, B, 2])
        sq_y = sb("sq_y", [P, G, B * JR])
        sq_junk = sq_y[:].rearrange("p g n -> p (g n)").bitcast(bf16)
        mul_junk = sb("mul_junk", [P, 2, 2, W])
        gamma = [sb("gamma1", [P, G]), sb("gamma2", [P, G])]
        beta = [sb("beta1", [P, G]), sb("beta2", [P, G])]
        lw1_sb = sb("lw1_sb", [P, CT // B, B, HID])
        lb1_sb = sb("lb1_sb", [P, HT])
        lb2_sb = sb("lb2_sb", [B, C])
        mean = sb("mean", [P, G, B])
        rstd = sb("rstd", [P, G, B])
        var, recip, tmp, mr, off = (sb(n, [P, G, B]) for n in ("var", "recip", "tmp", "mr", "off"))
        tap_sum = [sb("tap_sum1", [P, G]), sb("tap_sum2", [P, G])]
        part = sb("part", [P, G])
        bn_var, bn_recip, bn_rstd, bn_tmp = (sb(n, [P, G]) for n in ("bn_var", "bn_recip", "bn_rstd", "bn_tmp"))
        dot_p = sb("dot_p", [P, G, B])
        dot_c = sb("dot_c", [P, CT, B])
        hid = sb("hid", [P, HT, B])
        logit, prob = (mul_junk[0:B, i].rearrange("b h w -> b (h w)") for i in range(2))
        neg_max = sb("neg_max", [B, 1])
        exp_sum = sb("exp_sum", [B, 1])
        prob_c = sb("prob_c", [P, CT, B])
        scale = sb("scale", [P, G, B])
        shift = sb("shift", [P, G, B])

        ps_y = [pb("ps_y0", [P, B * W]), pb("ps_y1", [P, B * W])]
        ps_a = pb("ps_a", [P, 512])
        ps_b = pb("ps_b", [P, 512])
        ps_c = pb("ps_c", [P, 512])
        ps_d = pb("ps_d", [P, 512])

        y_dram = nc.dram_tensor("y_rows", [G, B, CG, W], f32, kind="Internal").ap()
        y_back = y_dram.rearrange("g b c (e j) -> (c e) g b j", e=E)

        x_loaded = [sem(f"x_loaded{s}") for s in range(S)]
        x_stored = [sem(f"x_stored{s}") for s in range(S)]
        w1_loaded = sem("w1_loaded")
        w2_loaded = [sem("w2_loaded0"), sem("w2_loaded1")]
        small_loaded = sem("small_loaded")
        lw2_loaded = sem("lw2_loaded")
        act_waited = sem("act_waited")
        sp_waited = sem("sp_waited")
        junk_free = sem("junk_free")
        squared = sem("squared")
        pe_read_x = sem("pe_read_x")
        masks_built = sem("masks_built")
        taps_ready = sem("taps_ready")
        bank_free = [sem("bank_free0"), sem("bank_free1")]
        y_sb_full = sem("y_sb_full")
        y_written = sem("y_written")
        y_loaded = sem("y_loaded")
        pool_step = sem("pool_step")
        dve_step = sem("dve_step")
        taps_summed = sem("taps_summed")
        filter_sums = sem("filter_sums")
        sums_written = sem("sums_written")
        group_moments = sem("group_moments")
        part_sums = sem("part_sums")
        channel_sums = sem("channel_sums")
        sqrt_asked = sem("sqrt_asked")
        sqrt_done = sem("sqrt_done")
        dots_ready = sem("dots_ready")
        dots_folded = sem("dots_folded")
        dots_copied = sem("dots_copied")
        hidden_ready = sem("hidden_ready")
        hidden_copied = sem("hidden_copied")
        logits_ready = sem("logits_ready")
        exp_asked = sem("exp_asked")
        exp_done = sem("exp_done")
        prob_ready = sem("prob_ready")
        prob_turned = sem("prob_turned")
        prob_copied = sem("prob_copied")
        prob_spread = sem("prob_spread")
        coefs_ready = sem("coefs_ready")
        dve_scaled = sem("dve_scaled")
        act_scaled = sem("act_scaled")

        block = ctx.enter_context(nc.Block())

        def bc(ap, n):
            return ap.unsqueeze(len(ap.shape)).to_broadcast(list(ap.shape) + [n])

        def wait_apart(engine, semaphore, value, passed):
            engine.wait_ge(semaphore, value)
            engine.sem_inc(passed, 1)

        @block.sync
        def _(sp):
            def load_unit(s, g):
                for b in range(B):
                    sp.dma_start(xs[:, s, b, :], x_v[g, :, b, (s % 2) * HALF:(s % 2 + 1) * HALF]
                                 ).then_inc(x_loaded[s], 16)

            def load_w2(i, g):
                sp.dma_start(w2_row[:, i, :], w2_v[g].unsqueeze(1).to_broadcast([CG, E, W])
                             ).then_inc(w2_loaded[i], 16)

            sp.dma_start(w1_sb, w1).then_inc(w1_loaded, 16)
            sp.dma_start(w2_sb[:], w2).then_inc(w1_loaded, 16)
            for s in range(S):
                if s % 2 == 0:
                    load_w2(s // 2, s // 2)
                load_unit(s, s // 2)
            for t, v in ((gamma[0], g1), (beta[0], b1), (gamma[1], g2), (beta[1], b2)):
                sp.dma_start(t[:], v.unsqueeze(1).to_broadcast([CG, E, G])).then_inc(small_loaded, 16)
            sp.dma_start(lw1_sb[:], lw1.rearrange("(t p b) o -> p t b o", p=P, b=B)).then_inc(small_loaded, 16)
            sp.dma_start(lb1_sb[:], lb1).then_inc(small_loaded, 16)
            for b in range(B):
                sp.dma_start(lb2_sb[b:b + 1, :], lb2).then_inc(small_loaded, 16)
            with sp.Fori(1, ROUNDS) as r:
                for s in range(S):
                    wait_apart(sp, pe_read_x, r * S + (s + 1 - S), sp_waited)
                    wait_apart(sp, junk_free, r * (S * PAIRS) + ((s + 1 - S) * PAIRS + 2), sp_waited)
                    wait_apart(sp, squared, r * (S * B) + ((s + 1 - S) * B + 1), sp_waited)
                    load_unit(s, r * 2 + s // 2)
                    if s % 2:
                        load_w2(s // 2, r * 2 + s // 2)
            sp.wait_ge(pe_read_x, UNITS)
            sp.wait_ge(junk_free, UNITS * PAIRS + 2)
            sp.wait_ge(taps_summed, 1)
            sp.wait_ge(y_written, 16 * G)
            sp.dma_start(lw2_sb[:], lw2.rearrange("(t p) c -> p t c", p=P)).then_inc(lw2_loaded, 16)
            with sp.Fori(0, ROUNDS - 1) as r:
                for s in range(S):
                    wait_apart(sp, x_stored[s], r * 16 + 16, sp_waited)
                    load_unit(s, r * 2 + s // 2)
            for s in range(S):
                sp.wait_ge(x_stored[s], 16 * ROUNDS)

        @block.gpsimd
        def _(pool):
            n = [0]

            def then_wait(ins):
                n[0] += 1
                ins.then_inc(pool_step, 1)
                pool.wait_ge(pool_step, n[0])

            def select(t, pattern, base, mult, op, fill):
                return nc.gpsimd.affine_select(out=t, in_=t, compare_op=op, fill=fill, base=base,
                                               pattern=pattern, channel_multiplier=mult)

            then_wait(nc.gpsimd.memset(own[:], 1.0))
            then_wait(select(own[:], [[-E, CG]], 0, 1, ALU.is_ge, 0.0))
            then_wait(select(own[:], [[E, CG]], E - 1, -1, ALU.is_ge, 0.0))
            for i in range(2):
                then_wait(nc.gpsimd.tensor_copy(
                    taps[:, i, :, CG:2 * CG], own[:].unsqueeze(1).to_broadcast([P, JR, CG])))
            pool.wait_ge(w1_loaded, 32)

            def build(i, g):
                nc.gpsimd.tensor_tensor(
                    taps[:, i, :, 0:CG], own[:].unsqueeze(1).to_broadcast([P, JR, CG]),
                    bc(w1_sb[:, g, :], CG), ALU.mult).then_inc(taps_ready, 1)

            build(0, 0)
            build(1, 1)
            with pool.Fori(1, G // 2) as r:
                for i in range(2):
                    pool.wait_ge(pe_read_x, r * 4 + (2 * i - 2))
                    build(i, r * 2 + i)

            then_wait(nc.gpsimd.tensor_copy(same[:].rearrange("p (c e) -> p c e", e=E), bc(own[:], E)))
            then_wait(nc.gpsimd.memset(fold[:], 0.0))
            then_wait(nc.gpsimd.tensor_copy(fold[:, 7 * CG:8 * CG], own[:]))
            then_wait(nc.gpsimd.memset(spread[:], 0.0))
            then_wait(select(spread[:].rearrange("p g (c e) -> p g c e", e=E),
                             [[-CG, GB], [-1, CG], [0, E]], 0, 1, ALU.not_equal, 1.0))
            then_wait(nc.gpsimd.memset(all_ones[:], 1.0 / GROUP_N))
            then_wait(nc.gpsimd.memset(quad_ones[:], 1.0 / GROUP_N))
            then_wait(select(quad_ones[:], [[-32, 4], [0, P]], -16, 1, ALU.is_ge, 0.0))
            then_wait(select(quad_ones[:], [[32, 4], [0, P]], 31, -1, ALU.is_ge, 0.0))
            then_wait(nc.gpsimd.memset(eye2[:], 0.0))
            select(eye2[:], [[-1, B]], 0, 1, ALU.not_equal, 1.0).then_inc(masks_built, 1)

        @block.tensor
        def _(pe):
            with pe.Fori(0, BLOCKS) as k:
                for gl in range(GB):
                    bank, q, i = gl // BANK_GROUPS, gl % BANK_GROUPS, gl % 2
                    pe.wait_ge(taps_ready, k * GB + gl + 1)
                    if q == 0:
                        pe.wait_ge(bank_free[bank], k + 1)
                    for hf in range(2):
                        s = (2 * gl + hf) % S
                        pe.wait_ge(x_loaded[s], k * (32 * 4) + 32 * ((2 * gl + hf) // S + 1))
                        for j in range(JH):
                            last = nc.tensor.matmul(
                                ps_y[bank][32 * q:32 * q + 32, :],
                                taps[:, i, hf * JH + j, :], xs[:, s, :, j * W:(j + 1) * W],
                                start=(hf == 0 and j == 0), stop=(hf == 1 and j == JH - 1))
                        last.then_inc(pe_read_x, 1)

            pe.wait_ge(masks_built, 1)
            pe.wait_ge(taps_summed, 1)
            for i in range(2):
                last = nc.tensor.matmul(ps_c[:, G * i:G * i + G], same[:], tap_sum[i][:],
                                        start=True, stop=True)
            last.then_inc(filter_sums, 1)
            pe.wait_ge(sums_written, 1)
            for q in range(BANK_GROUPS):
                nc.tensor.matmul(ps_a[:, 2 * 2 * BLOCKS * q:2 * 2 * BLOCKS * (q + 1)], quad_ones[:, q, :], y_sum[:],
                                 start=True, stop=True)
            nc.tensor.matmul(ps_b[:, 0:2 * G * B], all_ones[:], sq_sum[:],
                             start=True, stop=True).then_inc(group_moments, 1)
            for n in range(4):
                pe.wait_ge(part_sums, n + 1)
                nc.tensor.matmul(ps_d[:, G * n:G * n + G], same[:], part[:], start=True, stop=True
                                 ).then_inc(channel_sums, 1)
            pe.wait_ge(dots_ready, 1)
            by_group = dot_p[:].rearrange("p (t l) b -> p l t b", l=GB)
            for gl in range(GB):
                last = nc.tensor.matmul(ps_a[:, 0:CT * B], fold[:, (GB - 1 - gl) * CG:(GB - 1 - gl) * CG + P],
                                        by_group[:, gl], start=(gl == 0), stop=(gl == GB - 1))
            last.then_inc(dots_folded, 1)
            pe.wait_ge(small_loaded, 128)
            pe.wait_ge(dots_copied, 1)
            rows = dot_c[:].rearrange("p (q t) b -> p t b q", q=B)
            inputs = [(t, b) for t in range(CT // B) for b in range(B)]
            for o in range(HT):
                for t, b in inputs:
                    last = nc.tensor.matmul(ps_b[:, B * o:B * o + B], lw1_sb[:, t, b, o * P:(o + 1) * P],
                                            rows[:, t, b, :], start=((t, b) == inputs[0]),
                                            stop=((t, b) == inputs[-1]))
            last.then_inc(hidden_ready, 1)
            pe.wait_ge(hidden_copied, 1)
            pe.wait_ge(lw2_loaded, 16)
            for o in range(HT):
                last = nc.tensor.matmul(ps_c[0:B, :], hid[:, o, :], lw2_sb[:, o, :],
                                        start=(o == 0), stop=(o == HT - 1))
            last.then_inc(logits_ready, 1)
            pe.wait_ge(prob_ready, 1)
            for t in range(CT):
                last = nc.tensor.matmul(ps_d[:, B * t:B * t + B], prob[:, t * P:(t + 1) * P], eye2[:],
                                        start=True, stop=True)
            last.then_inc(prob_turned, 1)
            pe.wait_ge(prob_copied, 1)
            for gl in range(GB):
                last = nc.tensor.matmul(ps_a[:, gl * CT * B:(gl + 1) * CT * B], spread[:, gl, :],
                                        prob_c[:], start=True, stop=True)
            last.then_inc(prob_spread, 1)

        @block.scalar
        def _(act):
            act.sem_inc(squared, 1)
            act.sem_inc(bank_free[0], 1)
            act.sem_inc(bank_free[1], 1)
            with act.Fori(0, BLOCKS) as k:
                for gl in range(GB):
                    for hf in range(2):
                        s = (2 * gl + hf) % S
                        act.wait_ge(x_loaded[s], k * (32 * 4) + 32 * ((2 * gl + hf) // S + 1))
                        for b in range(B):
                            act.wait_ge(squared, k * (GB * 2 * B) + ((2 * gl + hf) * B + b + 1))
                            nc.scalar.activation(sq_junk, xs[:, s, b, :], ACT.Square,
                                                 accum_out=sq_sum[:, k * GB + gl, b, hf:hf + 1]
                                                 ).then_inc(squared, 1)
                    if gl % BANK_GROUPS == BANK_GROUPS - 1:
                        bank = gl // BANK_GROUPS
                        wait_apart(act, pe_read_x, k * (2 * GB) + 2 * (gl + 1), act_waited)
                        for b in range(B):
                            nc.scalar.activation(
                                y_sb[:, b, :], ps_y[bank][:, b * W:(b + 1) * W], ACT.Identity,
                                accum_out=y_sum[:, k * 2 + bank, b:b + 1]).then_inc(y_sb_full, 1)
                        act.wait_ge(y_sb_full, k * 4 + 2 * (bank + 1))
                        act.sem_inc(bank_free[bank], 1)
                        for q in range(BANK_GROUPS):
                            g = k * GB + (bank * BANK_GROUPS + q)
                            act.dma_start(y_dram[g].rearrange("b c w -> c b w"), y_sb[32 * q:32 * q + CG]
                                          ).then_inc(y_written, 16)
                        act.wait_ge(y_written, k * (16 * GB) + 16 * BANK_GROUPS * (bank + 1))
                        g = k * GB + bank * BANK_GROUPS
                        for q in range(BANK_GROUPS):
                            act.dma_start(y1[:, g + q], y_back[:, g + q]).then_inc(y_loaded, 16)
            act.drain().then_inc(sums_written, 1)

            for n, (to, of) in enumerate(((rstd, recip), (bn_rstd, bn_recip), (bn_rstd, bn_recip))):
                act.wait_ge(sqrt_asked, n + 1)
                nc.scalar.activation(to[:], of[:], ACT.Sqrt).then_inc(sqrt_done, 1)
            act.wait_ge(exp_asked, 1)
            nc.scalar.activation(prob, logit, ACT.Exp, bias=neg_max[:], accum_out=exp_sum[:]
                                 ).then_inc(exp_done, 1)

            def scale_unit(s, g, n):
                nc.scalar.activation(xs[:, s, 1, :], xs[:, s, 1, :], ACT.Identity,
                                     scale=scale[:, g, 1:2], bias=shift[:, g, 1:2]).then_inc(act_scaled, 1)
                act.wait_ge(act_scaled, n)
                act.wait_ge(dve_scaled, n)
                act.dma_start(out_v[g, :, :, (s % 2) * HALF:(s % 2 + 1) * HALF], xs[:, s]
                              ).then_inc(x_stored[s], 16)

            act.wait_ge(coefs_ready, 1)
            for s in range(S):
                scale_unit(s, G - S // 2 + s // 2, s + 1)
            with act.Fori(0, ROUNDS - 1) as r:
                for s in range(S):
                    wait_apart(act, x_loaded[s], r * 32 + 32 * (ROUNDS + 1), act_waited)
                    scale_unit(s, r * 2 + s // 2, r * S + (S + s + 1))

        @block.vector
        def _(dve):
            n = [0]

            def then_wait(ins):
                n[0] += 1
                ins.then_inc(dve_step, 1)
                dve.wait_ge(dve_step, n[0])

            dve.wait_ge(w1_loaded, 32)
            for t, w in zip(tap_sum, (w1_sb, w2_sb[:])):
                last = nc.vector.tensor_reduce(t[:], w, AX.X, ALU.add)
            last.then_inc(taps_summed, 1)
            dve.sem_inc(junk_free, 2)
            with dve.Fori(0, ROUNDS) as r:
                for s in range(S):
                    if s % 2 == 0:
                        dve.wait_ge(w2_loaded[s // 2], r * 16 + 16)
                    dve.wait_ge(x_loaded[s], r * 32 + 32)
                    for b in range(B):
                        for j in range(JH):
                            pair = s * PAIRS + (b * JH + j) // 2
                            if j % 2 == 0:
                                dve.wait_ge(junk_free, r * (S * PAIRS) + (pair + 1))
                            last = nc.vector.scalar_tensor_tensor(
                                out=mul_junk[:, pair % 2, j % 2, :], in0=xs[:, s, b, j * W:(j + 1) * W], scalar=1.0,
                                in1=w2_row[:, s // 2, :], op0=ALU.mult, op1=ALU.mult,
                                accum_out=y2[:, r * 2 + s // 2, b, (s % 2) * JH + j:(s % 2) * JH + j + 1])
                            if j % 2:
                                last.then_inc(junk_free, 1)

            dve.wait_ge(small_loaded, 128)

            def rsqrt(to, of, v, tmp, k):
                then_wait(nc.vector.reciprocal(of, v))
                nc.vector.sem_inc(sqrt_asked, 1)
                dve.wait_ge(sqrt_done, k)
                then_wait(nc.vector.reciprocal(tmp, to))
                then_wait(nc.vector.tensor_tensor(tmp, tmp, of, ALU.mult))
                then_wait(nc.vector.tensor_tensor(tmp, tmp, to, ALU.add))
                then_wait(nc.vector.tensor_scalar(to, tmp, 0.5, None, ALU.mult))

            dve.wait_ge(group_moments, 1)
            then_wait(nc.vector.tensor_copy(
                mean[:].rearrange("p (k q) b -> p q k b", q=BANK_GROUPS),
                ps_a[:, 0:G * B].rearrange("p (q k b) -> p q k b", q=BANK_GROUPS, b=B)))
            then_wait(nc.vector.tensor_reduce(var[:], ps_b[:, 0:2 * G * B].rearrange("p (g b h) -> p g b h", g=G, b=B),
                                              AX.X, ALU.add))
            then_wait(nc.vector.tensor_tensor(tmp[:], mean[:], mean[:], ALU.mult))
            then_wait(nc.vector.tensor_tensor(var[:], var[:], tmp[:], ALU.subtract))
            then_wait(nc.vector.tensor_scalar(var[:], var[:], 0.0, EPS, ALU.max, ALU.add))
            rsqrt(rstd[:], recip[:], var[:], tmp[:], 1)
            then_wait(nc.vector.tensor_tensor(mr[:], mean[:], rstd[:], ALU.mult))

            dve.wait_ge(filter_sums, 1)
            dve.wait_ge(y_loaded, 16 * G)
            for i in range(2):
                yi = y[i]
                chan = yi[:].rearrange("p g b j -> p g (b j)")
                then_wait(nc.vector.tensor_tensor(off[:], mr[:], bc(ps_c[:, G * i:G * i + G], B), ALU.mult))
                then_wait(nc.vector.tensor_tensor(yi[:], yi[:], bc(rstd[:], JR), ALU.mult))
                then_wait(nc.vector.tensor_tensor(yi[:], yi[:], bc(off[:], JR), ALU.subtract))
                nc.vector.tensor_reduce(part[:], chan, AX.X, ALU.add).then_inc(part_sums, 1)
                dve.wait_ge(channel_sums, 2 * i + 1)
                then_wait(nc.vector.tensor_scalar(bn_tmp[:], ps_d[:, 2 * G * i:2 * G * i + G], 1.0 / BN_N, None, ALU.mult))
                then_wait(nc.vector.tensor_tensor(chan, chan, bc(bn_tmp[:], B * JR), ALU.subtract))
                then_wait(nc.vector.tensor_tensor(sq_y[:], chan, chan, ALU.mult))
                nc.vector.tensor_reduce(part[:], sq_y[:], AX.X, ALU.add).then_inc(part_sums, 1)
                dve.wait_ge(channel_sums, 2 * i + 2)
                then_wait(nc.vector.tensor_scalar(bn_var[:], ps_d[:, 2 * G * i + G:2 * G * i + 2 * G], 1.0 / BN_N, EPS,
                                                  ALU.mult, ALU.add))
                rsqrt(bn_rstd[:], bn_recip[:], bn_var[:], bn_tmp[:], 2 + i)
                then_wait(nc.vector.tensor_tensor(bn_tmp[:], bn_rstd[:], gamma[i][:], ALU.mult))
                then_wait(nc.vector.tensor_tensor(chan, chan, bc(bn_tmp[:], B * JR), ALU.mult))
                then_wait(nc.vector.tensor_tensor(chan, chan, bc(beta[i][:], B * JR), ALU.add))
            flat = [t[:].rearrange("p g b j -> p (g b j)") for t in y]
            then_wait(nc.vector.tensor_scalar(flat[1], flat[1], 0.0, None, ALU.max))
            then_wait(nc.vector.scalar_tensor_tensor(out=flat[0], in0=flat[0], scalar=0.0, in1=flat[1],
                                                     op0=ALU.max, op1=ALU.mult))
            nc.vector.tensor_reduce(dot_p[:], y1[:], AX.X, ALU.add).then_inc(dots_ready, 1)

            dve.wait_ge(dots_folded, 1)
            nc.vector.tensor_copy(dot_c[:], ps_a[:, 0:CT * B].rearrange("p (t b) -> p t b", b=B)
                                  ).then_inc(dots_copied, 1)
            dve.wait_ge(hidden_ready, 1)
            nc.vector.tensor_tensor(hid[:], ps_b[:, 0:HT * B].rearrange("p (o b) -> p o b", b=B),
                                    bc(lb1_sb[:], B), ALU.add).then_inc(hidden_copied, 1)
            dve.wait_ge(logits_ready, 1)
            then_wait(nc.vector.tensor_tensor(logit, ps_c[0:B, :], lb2_sb[:], ALU.add))
            then_wait(nc.vector.reduce_max(neg_max[:], logit, AX.X))
            nc.vector.tensor_scalar(neg_max[:], neg_max[:], -1.0, None, ALU.mult).then_inc(exp_asked, 1)
            dve.wait_ge(exp_done, 1)
            then_wait(nc.vector.reciprocal(exp_sum[:], exp_sum[:]))
            nc.vector.tensor_scalar(prob, prob, exp_sum[:], None, ALU.mult).then_inc(prob_ready, 1)
            dve.wait_ge(prob_turned, 1)
            nc.vector.tensor_copy(prob_c[:], ps_d[:, 0:CT * B].rearrange("p (t b) -> p t b", b=B)
                                  ).then_inc(prob_copied, 1)
            dve.wait_ge(prob_spread, 1)
            then_wait(nc.vector.tensor_tensor(
                tmp[:].rearrange("p (t l) b -> p t l b", l=GB), rstd[:].rearrange("p (t l) b -> p t l b", l=GB),
                ps_a[:, 0:G * B].rearrange("p (l t b) -> p t l b", l=GB, b=B), ALU.mult))
            then_wait(nc.vector.tensor_scalar(scale[:], tmp[:], 1.0, None, ALU.add))
            then_wait(nc.vector.tensor_tensor(tmp[:], tmp[:], mean[:], ALU.mult))
            then_wait(nc.vector.tensor_scalar(shift[:], tmp[:], -1.0, None, ALU.mult))
            nc.vector.sem_inc(coefs_ready, 1)

            def scale_unit(s, g):
                nc.vector.tensor_scalar(xs[:, s, 0, :], xs[:, s, 0, :], scale[:, g, 0:1], shift[:, g, 0:1],
                                        ALU.mult, ALU.add).then_inc(dve_scaled, 1)

            for s in range(S):
                scale_unit(s, G - S // 2 + s // 2)
            with dve.Fori(0, ROUNDS - 1) as r:
                for s in range(S):
                    dve.wait_ge(x_loaded[s], r * 32 + 32 * (ROUNDS + 1))
                    scale_unit(s, r * 2 + s // 2)


def kernel(**inputs):
    import numpy as np
    import concourse.bacc as bacc
    from concourse.bass_utils import run_bass_kernel_spmd

    a = {k.replace("L0_conv_", ""): np.asarray(v) for k, v in inputs.items()}

    def by_partition(w):
        return w.reshape(G, CG, E, -1).transpose(1, 2, 0, 3).reshape(P, G, -1)

    laid = {
        "x": a["x"],
        "w1": by_partition(a["w1"].reshape(C, H)),
        "w2": by_partition(a["w2"].reshape(C, W)),
        **{n: a[n].reshape(G, CG).T for n in ("g1", "b1", "g2", "b2")},
        "w2_rows": a["w2"].reshape(C, W),
        "lw1": a["lw1"].T, "lb1": a["lb1"].reshape(HT, P).T,
        "lw2": a["lw2"].T, "lb2": a["lb2"].reshape(1, C),
    }
    nc = bacc.Bacc("TRN2", target_bir_lowering=False, num_devices=1)
    arrays, args = {}, []
    for name, v in laid.items():
        arrays[f"in_{name}"] = np.ascontiguousarray(v)
        args.append(nc.dram_tensor(f"in_{name}", v.shape, mybir.dt.from_np(v.dtype), kind="ExternalInput").ap())
    out = nc.dram_tensor("out_0", (B, C, H, W), mybir.dt.float32, kind="ExternalOutput").ap()
    conv_preact(nc, *args, out)
    r = run_bass_kernel_spmd(nc, [arrays], core_ids=[0])
    return r.results[0]["out_0"]
```

```python
import concourse.bass as bass
from concourse import mybir
from contextlib import ExitStack

P = 128
B, C, H, W = 2, 512, 256, 256
G = 32
CG = C // G
E = P // CG
JR = H // E
JH = JR // 2
S = 4
UNITS = 2 * G
ROUNDS = UNITS // S
GB = 8
BLOCKS = G // GB
BANK_GROUPS = 4
PAIRS = B * JH // 2
HID = 2 * C
HT = HID // P
CT = C // P
GROUP_N = CG * H * W
BN_STEPS = 17
BN_N = B * W
EPS = 1e-5


def conv_preact(nc, x, w1, w2, g1, b1, g2, b2, w2_rows, lw1, lb1, lw2, lb2, out):
    f32 = mybir.dt.float32
    bf16 = mybir.dt.bfloat16
    ALU = mybir.AluOpType
    ACT = mybir.ActivationFunctionType
    AX = mybir.AxisListType

    x_v = x.rearrange("b (g c) (e j) w -> g (c e) b (j w)", c=CG, e=E)
    out_v = out.rearrange("b (g c) (e j) w -> g (c e) b (j w)", c=CG, e=E)
    HALF = JH * W

    with ExitStack() as ctx:
        def sb(name, shape, dt=f32):
            return ctx.enter_context(nc.sbuf_tensor(name, shape, dt))

        def pb(name, shape):
            return ctx.enter_context(nc.psum_tensor(name, shape, f32))

        def sem(name):
            return ctx.enter_context(nc.semaphore(name))

        xs = sb("xs", [P, S, B, HALF])
        lw2_sb = sb("lw2_sb", [P, HT, C])
        lw2_room = lw2_sb[:].rearrange("p o c -> p (o c)")
        taps = lw2_room[:, 0:2048].rearrange("p (i j m) -> p i j m", i=2, m=2 * CG)
        w1_sb = lw2_room[:, 2048:3072].rearrange("p (g j) -> p g j", g=G)
        y_sb = lw2_room[:, 3584:4096].rearrange("p (b w) -> p b w", b=B)
        lw1_sb = sb("lw1_sb", [P, CT // B, B, HID])
        lw1_room = lw1_sb[:].rearrange("p t b o -> p (t b o)")
        w2_sb = lw1_room[:, 0:1024].rearrange("p (g j) -> p g j", g=G)
        w2_c = lw1_room[:, 1024:2048].rearrange("p (t w) -> p t w", t=CT)
        sq_junk = lw1_room[:, 2048:4096].bitcast(bf16)
        own = sb("own", [P, CG])
        same = sb("same", [P, P])
        fold = sb("fold", [P, 15 * CG])
        spread = sb("spread", [P, GB, P])
        quad_ones = sb("quad_ones", [P, 4, P])
        all_ones = sb("all_ones", [P, P])
        eye2 = sb("eye2", [B, B])
        y1 = sb("y1", [P, G, B, JR])
        y2 = sb("y2", [P, G, B, JR])
        z = sb("z", [P, 2, GB, B * JR])
        zz = sb("zz", [P, 2, GB, B * JR])
        y_sum = sb("y_sum", [P, 2 * BLOCKS, B])
        sq_sum = sb("sq_sum", [P, G, B, 2])
        mul_junk = sb("mul_junk", [P, 2, 2, W])
        gamma = sb("gamma", [P, 2, G])
        beta = sb("beta", [P, 2, G])
        lb1_sb = sb("lb1_sb", [P, HT])
        lb2_sb = sb("lb2_sb", [B, C])
        rstd = sb("rstd", [P, G, B])
        mean_rstd = sb("mean_rstd", [P, G, B])
        mean, var, square, rstd_k, mr_k = (sb(n, [P, GB, B]) for n in ("mean", "var", "square", "rstd_k", "mr_k"))
        off = sb("off", [P, 2, GB, B])
        tap_part = sb("tap_part", [P, 2, G])
        tap_sum = sb("tap_sum", [P, 2, G])
        part = sb("part", [P, 2, GB])
        bn_mean, bn_var, bn_rstd, bn_scale = (sb(n, [P, 2, GB]) for n in ("bn_mean", "bn_var", "bn_rstd", "bn_scale"))
        minus_half = sb("minus_half", [P, 2 * GB])
        dot_p = sb("dot_p", [P, G, B])
        dot_c = sb("dot_c", [P, CT, B])
        hid = sb("hid", [P, HT, B])
        logit, prob = (mul_junk[0:B, i].rearrange("b h w -> b (h w)") for i in range(2))
        neg_max = sb("neg_max", [B, 1])
        exp_sum = sb("exp_sum", [B, 1])
        prob_c = sb("prob_c", [P, CT, B])
        scale = sb("scale", [P, G, B])
        tmp = sb("tmp", [P, G, B])
        shift = sb("shift", [P, G, B])

        ps_w2 = [pb("ps_w2_0", [P, 512]), pb("ps_w2_1", [P, 512])]
        ps_y = [pb("ps_y0", [P, B * W]), pb("ps_y1", [P, B * W])]
        ps_a = pb("ps_a", [P, 512])
        ps_b = pb("ps_b", [P, 512])
        ps_c = pb("ps_c", [P, 512])
        ps_d = pb("ps_d", [P, 512])

        y_dram = nc.dram_tensor("y_rows", [G, B, CG, W], f32, kind="Internal").ap()
        y_back = y_dram.rearrange("g b c (e j) -> (c e) g b j", e=E)

        x_loaded = [sem(f"x_loaded{s}") for s in range(S)]
        x_stored = [sem(f"x_stored{s}") for s in range(S)]
        w1_loaded = sem("w1_loaded")
        w2_ready = sem("w2_ready")
        small_loaded = sem("small_loaded")
        lw1_loaded = sem("lw1_loaded")
        lw2_loaded = sem("lw2_loaded")
        act_waited = sem("act_waited")
        sp_waited = sem("sp_waited")
        junk_free = sem("junk_free")
        squared = sem("squared")
        pe_read_x = sem("pe_read_x")
        masks_built = sem("masks_built")
        taps_ready = sem("taps_ready")
        bank_free = [sem("bank_free0"), sem("bank_free1")]
        y_sb_full = sem("y_sb_full")
        y_written = sem("y_written")
        y_loaded = sem("y_loaded")
        pool_step = sem("pool_step")
        dve_step = sem("dve_step")
        taps_summed = sem("taps_summed")
        filter_sums = sem("filter_sums")
        sums_written = sem("sums_written")
        group_moments = sem("group_moments")
        part_sums = sem("part_sums")
        channel_sums = sem("channel_sums")
        var_ready = sem("var_ready")
        rstd_ready = sem("rstd_ready")
        channels_built = sem("channels_built")
        bn_step = sem("bn_step")
        bn_waited = sem("bn_waited")
        pool_waited = sem("pool_waited")
        dots_ready = sem("dots_ready")
        dots_folded = sem("dots_folded")
        dots_copied = sem("dots_copied")
        hidden_ready = sem("hidden_ready")
        hidden_copied = sem("hidden_copied")
        logits_ready = sem("logits_ready")
        exp_asked = sem("exp_asked")
        exp_done = sem("exp_done")
        prob_ready = sem("prob_ready")
        prob_turned = sem("prob_turned")
        prob_copied = sem("prob_copied")
        prob_spread = sem("prob_spread")
        coefs_ready = sem("coefs_ready")
        dve_scaled = sem("dve_scaled")
        act_scaled = sem("act_scaled")

        block = ctx.enter_context(nc.Block())

        def bc(ap, n):
            return ap.unsqueeze(len(ap.shape)).to_broadcast(list(ap.shape) + [n])

        def wait_apart(engine, semaphore, value, passed):
            engine.wait_ge(semaphore, value)
            engine.sem_inc(passed, 1)

        @block.sync
        def _(sp):
            def load_unit(s, g):
                for b in range(B):
                    sp.dma_start(xs[:, s, b, :], x_v[g, :, b, (s % 2) * HALF:(s % 2 + 1) * HALF]
                                 ).then_inc(x_loaded[s], 16)

            sp.dma_start(w1_sb, w1).then_inc(w1_loaded, 16)
            sp.dma_start(w2_sb, w2).then_inc(w1_loaded, 16)
            sp.dma_start(w2_c, w2_rows.rearrange("(t p) w -> p t w", p=P)).then_inc(w1_loaded, 16)
            for s in range(S):
                load_unit(s, s // 2)
            for t, i, v in ((gamma, 0, g1), (beta, 0, b1), (gamma, 1, g2), (beta, 1, b2)):
                sp.dma_start(t[:, i], v.unsqueeze(1).to_broadcast([CG, E, G])).then_inc(small_loaded, 16)
            sp.dma_start(lb1_sb[:], lb1).then_inc(small_loaded, 16)
            for b in range(B):
                sp.dma_start(lb2_sb[b:b + 1, :], lb2).then_inc(small_loaded, 16)
            with sp.Fori(1, ROUNDS) as r:
                for s in range(S):
                    wait_apart(sp, pe_read_x, r * S + (s + 1 - S), sp_waited)
                    wait_apart(sp, junk_free, r * (S * PAIRS) + ((s + 1 - S) * PAIRS + 2), sp_waited)
                    wait_apart(sp, squared, r * (S * B) + ((s + 1 - S) * B + 1), sp_waited)
                    load_unit(s, r * 2 + s // 2)
            sp.wait_ge(taps_summed, 1)
            sp.wait_ge(w2_ready, G)
            sp.wait_ge(squared, UNITS * B + 1)
            sp.dma_start(lw1_sb[:], lw1.rearrange("(t p b) o -> p t b o", p=P, b=B)).then_inc(lw1_loaded, 16)
            sp.wait_ge(pe_read_x, UNITS)
            sp.wait_ge(y_written, 16 * G)
            sp.dma_start(lw2_sb[:], lw2.rearrange("(t p) c -> p t c", p=P)).then_inc(lw2_loaded, 16)
            with sp.Fori(0, ROUNDS - 1) as r:
                for s in range(S):
                    wait_apart(sp, x_stored[s], r * 16 + 16, sp_waited)
                    load_unit(s, r * 2 + s // 2)
            for s in range(S):
                sp.wait_ge(x_stored[s], 16 * ROUNDS)

        @block.gpsimd
        def _(pool):
            n = [0]

            def then_wait(ins):
                n[0] += 1
                ins.then_inc(pool_step, 1)
                pool.wait_ge(pool_step, n[0])

            def select(t, pattern, base, mult, op, fill):
                return nc.gpsimd.affine_select(out=t, in_=t, compare_op=op, fill=fill, base=base,
                                               pattern=pattern, channel_multiplier=mult)

            then_wait(nc.gpsimd.memset(own[:], 1.0))
            then_wait(select(own[:], [[-E, CG]], 0, 1, ALU.is_ge, 0.0))
            then_wait(select(own[:], [[E, CG]], E - 1, -1, ALU.is_ge, 0.0))
            then_wait(nc.gpsimd.memset(spread[:], 0.0))
            then_wait(select(spread[:].rearrange("p g (c e) -> p g c e", e=E),
                             [[-CG, GB], [-1, CG], [0, E]], 0, 1, ALU.not_equal, 1.0))
            then_wait(nc.gpsimd.tensor_copy(same[:].rearrange("p (c e) -> p c e", e=E), bc(own[:], E)))
            pool.sem_inc(channels_built, 1)
            for i in range(2):
                then_wait(nc.gpsimd.tensor_copy(
                    taps[:, i, :, CG:2 * CG], own[:].unsqueeze(1).to_broadcast([P, JR, CG])))
            pool.wait_ge(w1_loaded, 48)

            def build(g, i):
                nc.gpsimd.tensor_tensor(
                    taps[:, i, :, 0:CG], own[:].unsqueeze(1).to_broadcast([P, JR, CG]),
                    bc(w1_sb[:, g, :], CG), ALU.mult).then_inc(taps_ready, 1)

            def build_behind(g, i):
                wait_apart(pool, pe_read_x, g * 2 - 2, pool_waited)
                build(g, i)

            def rsqrts(kb, n):
                to, of = ((rstd_k, var), (bn_rstd, bn_var))[n]
                wait_apart(pool, var_ready, kb * 2 + (n + 1), pool_waited)
                nc.gpsimd.tensor_tensor(to[:].rearrange("p a b -> p (a b)"), of[:].rearrange("p a b -> p (a b)"),
                                        minus_half[:], ALU.pow).then_inc(rstd_ready, 1)

            build(0, 0)
            build(1, 1)
            then_wait(nc.gpsimd.memset(minus_half[:], -0.5))
            then_wait(nc.gpsimd.memset(fold[:], 0.0))
            then_wait(nc.gpsimd.tensor_copy(fold[:, 7 * CG:8 * CG], own[:]))
            then_wait(nc.gpsimd.memset(all_ones[:], 1.0 / GROUP_N))
            then_wait(nc.gpsimd.memset(quad_ones[:], 1.0 / GROUP_N))
            then_wait(select(quad_ones[:], [[-32, 4], [0, P]], -16, 1, ALU.is_ge, 0.0))
            then_wait(select(quad_ones[:], [[32, 4], [0, P]], 31, -1, ALU.is_ge, 0.0))
            then_wait(nc.gpsimd.memset(eye2[:], 0.0))
            then_wait(select(eye2[:], [[-1, B]], 0, 1, ALU.not_equal, 1.0))
            pool.sem_inc(masks_built, 1)
            for g in range(2, GB + 2):
                build_behind(g, g % 2)

            def block_behind(k, ahead):
                for gl in range(2, GB + ahead):
                    if gl == 4:
                        rsqrts(k - 1, 0)
                    if gl == GB:
                        rsqrts(k - 1, 1)
                    build_behind(k * GB + gl, gl % 2)
                if not ahead:
                    rsqrts(k - 1, 1)

            with pool.Fori(1, BLOCKS - 1) as k:
                block_behind(k, 2)
            block_behind(BLOCKS - 1, 0)
            for n in range(2):
                rsqrts(BLOCKS - 1, n)

        @block.tensor
        def _(pe):
            def spread_w2(k, gl):
                if not (type(k) is int and k * GB + gl < 2):
                    pe.wait_ge(junk_free, k * (2 * GB * PAIRS) + ((gl - 1) * 2 * PAIRS + 2))
                nc.tensor.matmul(ps_w2[gl % 2][:, 0:W], spread[:, gl, :], w2_c[:, k, :],
                                 start=True, stop=True).then_inc(w2_ready, 1)

            def filter_group(k, gl):
                bank, q, i = gl // BANK_GROUPS, gl % BANK_GROUPS, gl % 2
                if gl == 0:
                    spread_w2(k, 0)
                pe.wait_ge(taps_ready, k * GB + (gl + 1))
                if q == 0:
                    pe.wait_ge(bank_free[bank], k + 1)
                for hf in range(2):
                    s = (2 * gl + hf) % S
                    pe.wait_ge(x_loaded[s], k * (32 * 4) + 32 * ((2 * gl + hf) // S + 1))
                    for j in range(JH):
                        last = nc.tensor.matmul(
                            ps_y[bank][32 * q:32 * q + 32, :],
                            taps[:, i, hf * JH + j, :], xs[:, s, :, j * W:(j + 1) * W],
                            start=(hf == 0 and j == 0), stop=(hf == 1 and j == JH - 1))
                    last.then_inc(pe_read_x, 1)
                    if hf == 0 and gl < GB - 1:
                        spread_w2(k, gl + 1)

            def moments(kb):
                pe.wait_ge(sums_written, kb + 1)
                for q in range(BANK_GROUPS):
                    nc.tensor.matmul(ps_a[:, 2 * B * q:2 * B * (q + 1)], quad_ones[:, q, :],
                                     y_sum[:, bass.ds(kb * 2, 2), :], start=True, stop=True)
                nc.tensor.matmul(ps_a[:, GB * B:3 * GB * B], all_ones[:], sq_sum[:, bass.ds(kb * GB, GB)],
                                 start=True, stop=True).then_inc(group_moments, 1)

            def channel_sum(kb, n):
                pe.wait_ge(part_sums, kb * 2 + (n + 1))
                nc.tensor.matmul((ps_b, ps_c)[n][:, 0:2 * GB], same[:], part[:], start=True, stop=True
                                 ).then_inc(channel_sums, 1)

            pe.wait_ge(channels_built, 1)
            pe.wait_ge(w1_loaded, 48)
            pe.wait_ge(taps_summed, 1)
            nc.tensor.matmul(ps_d[:, 0:2 * G], same[:], tap_part[:], start=True, stop=True).then_inc(filter_sums, 1)
            for gl in range(GB):
                filter_group(0, gl)
            pe.wait_ge(masks_built, 1)
            with pe.Fori(1, BLOCKS) as k:
                for gl in range(GB):
                    filter_group(k, gl)
                    if gl == 0:
                        moments(k - 1)
                    if gl == 4:
                        channel_sum(k - 1, 0)
                    if gl == 5:
                        channel_sum(k - 1, 1)
            moments(BLOCKS - 1)
            channel_sum(BLOCKS - 1, 0)
            channel_sum(BLOCKS - 1, 1)
            pe.wait_ge(dots_ready, BLOCKS)
            by_group = dot_p[:].rearrange("p (t l) b -> p l t b", l=GB)
            for gl in range(GB):
                last = nc.tensor.matmul(ps_a[:, 0:CT * B], fold[:, (GB - 1 - gl) * CG:(GB - 1 - gl) * CG + P],
                                        by_group[:, gl], start=(gl == 0), stop=(gl == GB - 1))
            last.then_inc(dots_folded, 1)
            pe.wait_ge(lw1_loaded, 16)
            pe.wait_ge(dots_copied, 1)
            rows = dot_c[:].rearrange("p (q t) b -> p t b q", q=B)
            inputs = [(t, b) for t in range(CT // B) for b in range(B)]
            for o in range(HT):
                for t, b in inputs:
                    last = nc.tensor.matmul(ps_b[:, B * o:B * o + B], lw1_sb[:, t, b, o * P:(o + 1) * P],
                                            rows[:, t, b, :], start=((t, b) == inputs[0]),
                                            stop=((t, b) == inputs[-1]))
            last.then_inc(hidden_ready, 1)
            pe.wait_ge(hidden_copied, 1)
            pe.wait_ge(lw2_loaded, 16)
            for o in range(HT):
                last = nc.tensor.matmul(ps_c[0:B, :], hid[:, o, :], lw2_sb[:, o, :],
                                        start=(o == 0), stop=(o == HT - 1))
            last.then_inc(logits_ready, 1)
            pe.wait_ge(prob_ready, 1)
            for t in range(CT):
                last = nc.tensor.matmul(ps_d[:, B * t:B * t + B], prob[:, t * P:(t + 1) * P], eye2[:],
                                        start=True, stop=True)
            last.then_inc(prob_turned, 1)
            pe.wait_ge(prob_copied, 1)
            for gl in range(GB):
                last = nc.tensor.matmul(ps_a[:, gl * CT * B:(gl + 1) * CT * B], spread[:, gl, :],
                                        prob_c[:], start=True, stop=True)
            last.then_inc(prob_spread, 1)

        @block.scalar
        def _(act):
            act.sem_inc(squared, 1)
            act.sem_inc(bank_free[0], 1)
            act.sem_inc(bank_free[1], 1)

            def square_group(k, gl):
                for hf in range(2):
                    s = (2 * gl + hf) % S
                    act.wait_ge(x_loaded[s], k * (32 * 4) + 32 * ((2 * gl + hf) // S + 1))
                    for b in range(B):
                        act.wait_ge(squared, k * (GB * 2 * B) + ((2 * gl + hf) * B + b + 1))
                        nc.scalar.activation(sq_junk, xs[:, s, b, :], ACT.Square,
                                             accum_out=sq_sum[:, k * GB + gl, b, hf:hf + 1]
                                             ).then_inc(squared, 1)

            def store_bank(k, bank):
                wait_apart(act, pe_read_x, k * (2 * GB) + 2 * BANK_GROUPS * (bank + 1), act_waited)
                for b in range(B):
                    nc.scalar.activation(
                        y_sb[:, b, :], ps_y[bank][:, b * W:(b + 1) * W], ACT.Identity,
                        accum_out=y_sum[:, k * 2 + bank, b:b + 1]).then_inc(y_sb_full, 1)
                act.wait_ge(y_sb_full, k * 4 + 2 * (bank + 1))
                if bank:
                    act.wait_ge(squared, k * (GB * 2 * B) + (GB * 2 * B + 1))
                    act.sem_inc(sums_written, 1)
                act.sem_inc(bank_free[bank], 1)
                for q in range(BANK_GROUPS):
                    act.dma_start(y_dram[k * GB + (bank * BANK_GROUPS + q)].rearrange("b c w -> c b w"),
                                  y_sb[32 * q:32 * q + CG]).then_inc(y_written, 16)

            def fetch_bank(n):
                act.wait_ge(y_written, n * (16 * BANK_GROUPS) + 16 * BANK_GROUPS)
                if type(n) is not int or n:
                    act.wait_ge(y_loaded, n * (16 * BANK_GROUPS))
                for q in range(BANK_GROUPS):
                    g = n * BANK_GROUPS + q
                    act.dma_start(y1[:, g], y_back[:, g]).then_inc(y_loaded, 16)

            def first_pass_block(k):
                for gl in range(GB):
                    square_group(k, gl)
                    if gl == 1 and not (type(k) is int):
                        fetch_bank(k * 2 - 1)
                    if gl == 3:
                        store_bank(k, 0)
                    if gl == 5:
                        fetch_bank(k * 2)
                store_bank(k, 1)

            first_pass_block(0)
            with act.Fori(1, BLOCKS) as k:
                first_pass_block(k)
            fetch_bank(2 * BLOCKS - 1)
            act.wait_ge(exp_asked, 1)
            nc.scalar.activation(prob, logit, ACT.Exp, bias=neg_max[:], accum_out=exp_sum[:]
                                 ).then_inc(exp_done, 1)

            def scale_unit(s, g, n):
                nc.scalar.activation(xs[:, s, 1, :], xs[:, s, 1, :], ACT.Identity,
                                     scale=scale[:, g, 1:2], bias=shift[:, g, 1:2]).then_inc(act_scaled, 1)
                act.wait_ge(act_scaled, n)
                act.wait_ge(dve_scaled, n)
                act.dma_start(out_v[g, :, :, (s % 2) * HALF:(s % 2 + 1) * HALF], xs[:, s]
                              ).then_inc(x_stored[s], 16)

            act.wait_ge(coefs_ready, 1)
            for s in range(S):
                scale_unit(s, G - S // 2 + s // 2, s + 1)
            with act.Fori(0, ROUNDS - 1) as r:
                for s in range(S):
                    wait_apart(act, x_loaded[s], r * 32 + 32 * (ROUNDS + 1), act_waited)
                    scale_unit(s, r * 2 + s // 2, r * S + (S + s + 1))

        @block.vector
        def _(dve):
            n = [0]

            def then_wait(ins):
                n[0] += 1
                ins.then_inc(dve_step, 1)
                dve.wait_ge(dve_step, n[0])

            dve.wait_ge(w1_loaded, 48)
            for i, w in enumerate((w1_sb, w2_sb)):
                last = nc.vector.tensor_reduce(tap_part[:, i], w, AX.X, ALU.add)
            last.then_inc(taps_summed, 1)
            dve.sem_inc(junk_free, 2)

            def filter_group(g, odd):
                dve.wait_ge(w2_ready, g + 1)
                for hf in range(2):
                    s = 2 * odd + hf
                    dve.wait_ge(x_loaded[s], g * 16 + (32 - 16 * odd))
                    for b in range(B):
                        for j in range(JH):
                            pair = hf * PAIRS + (b * JH + j) // 2
                            if j % 2 == 0:
                                dve.wait_ge(junk_free, g * (2 * PAIRS) + (pair + 1))
                            row = hf * JH + j
                            last = nc.vector.scalar_tensor_tensor(
                                out=mul_junk[:, pair % 2, j % 2, :], in0=xs[:, s, b, j * W:(j + 1) * W], scalar=1.0,
                                in1=ps_w2[odd][:, 0:W], op0=ALU.mult, op1=ALU.mult,
                                accum_out=y2[:, g, b, row:row + 1])
                            if j % 2:
                                last.then_inc(junk_free, 1)

            steps = [0]

            def chain(kb, ins):
                steps[0] += 1
                ins.then_inc(bn_step, 1)
                dve.wait_ge(bn_step, kb * BN_STEPS + steps[0])

            def chain_apart(kb, ins):
                steps[0] += 1
                ins.then_inc(bn_step, 1)
                wait_apart(dve, bn_step, kb * BN_STEPS + steps[0], bn_waited)

            def group_statistics(kb):
                steps[0] = 0
                dve.wait_ge(group_moments, kb + 1)
                chain(kb, nc.vector.tensor_copy(mean[:].rearrange("p (k q) b -> p q k b", q=BANK_GROUPS),
                                                ps_a[:, 0:GB * B].rearrange("p (q k b) -> p q k b", q=BANK_GROUPS, b=B)))
                chain(kb, nc.vector.tensor_reduce(var[:], ps_a[:, GB * B:3 * GB * B].rearrange(
                    "p (g b h) -> p g b h", b=B, h=2), AX.X, ALU.add))
                chain(kb, nc.vector.tensor_tensor(square[:], mean[:], mean[:], ALU.mult))
                chain(kb, nc.vector.tensor_tensor(var[:], var[:], square[:], ALU.subtract))
                nc.vector.tensor_scalar(var[:], var[:], 0.0, EPS, ALU.max, ALU.add).then_inc(var_ready, 1)

            def normalised_filters(kb):
                block_of = bass.ds(kb * GB, GB)
                dve.wait_ge(rstd_ready, kb * 2 + 1)
                chain_apart(kb, nc.vector.tensor_tensor(mr_k[:], mean[:], rstd_k[:], ALU.mult))
                nc.vector.tensor_copy(rstd[:, block_of], rstd_k[:])
                nc.vector.tensor_copy(mean_rstd[:, block_of], mr_k[:])
                chain(kb, nc.vector.tensor_tensor(off[:], mr_k[:].unsqueeze(1).to_broadcast([P, 2, GB, B]),
                                                  bc(tap_sum[:, :, block_of], B), ALU.mult))
                wait_apart(dve, y_loaded, kb * (16 * GB) + 16 * GB, bn_waited)
                for i, yi in enumerate((y1, y2)):
                    chain(kb, nc.vector.tensor_tensor(z[:, i].rearrange("p g (b j) -> p g b j", b=B),
                                                      yi[:, block_of], bc(rstd_k[:], JR), ALU.mult))
                by_batch = z[:].rearrange("p i g (b j) -> p (i g b) j", b=B)
                chain(kb, nc.vector.tensor_tensor(by_batch, by_batch, bc(off[:].rearrange("p i g b -> p (i g b)"), JR),
                                                  ALU.subtract))
                nc.vector.tensor_reduce(part[:], z[:], AX.X, ALU.add).then_inc(part_sums, 1)

            channels = z[:].rearrange("p i g n -> p (i g) n")
            squares = zz[:].rearrange("p i g n -> p (i g) n")

            def flat(t):
                return t.rearrange("p i g -> p (i g)")

            def centred(kb):
                dve.wait_ge(channel_sums, kb * 2 + 1)
                chain(kb, nc.vector.tensor_scalar(flat(bn_mean[:]), ps_b[:, 0:2 * GB], 1.0 / BN_N, None, ALU.mult))
                chain(kb, nc.vector.tensor_tensor(channels, channels, bc(flat(bn_mean[:]), B * JR), ALU.subtract))
                chain(kb, nc.vector.tensor_tensor(squares, channels, channels, ALU.mult))
                nc.vector.tensor_reduce(part[:], zz[:], AX.X, ALU.add).then_inc(part_sums, 1)

            def channel_variance(kb):
                dve.wait_ge(channel_sums, kb * 2 + 2)
                nc.vector.tensor_scalar(flat(bn_var[:]), ps_c[:, 0:2 * GB], 1.0 / BN_N, EPS,
                                        ALU.mult, ALU.add).then_inc(var_ready, 1)

            def dot_products(kb):
                block_of = bass.ds(kb * GB, GB)
                dve.wait_ge(rstd_ready, kb * 2 + 2)
                chain(kb, nc.vector.tensor_tensor(bn_scale[:], bn_rstd[:], gamma[:, :, block_of], ALU.mult))
                chain(kb, nc.vector.tensor_tensor(channels, channels, bc(flat(bn_scale[:]), B * JR), ALU.mult))
                chain(kb, nc.vector.tensor_tensor(z[:], z[:], bc(beta[:, :, block_of], B * JR), ALU.add))
                chain(kb, nc.vector.tensor_scalar(z[:, 1], z[:, 1], 0.0, None, ALU.max))
                chain_apart(kb, nc.vector.scalar_tensor_tensor(out=zz[:, 0], in0=z[:, 0], scalar=0.0, in1=z[:, 1],
                                                               op0=ALU.max, op1=ALU.mult))
                nc.vector.tensor_reduce(dot_p[:, block_of], zz[:, 0].rearrange("p g (b j) -> p g b j", b=B),
                                        AX.X, ALU.add).then_inc(dots_ready, 1)
                assert steps[0] == BN_STEPS, steps

            after_group = {1: group_statistics, 4: normalised_filters, 5: centred, 6: channel_variance, 7: dot_products}
            with dve.Fori(0, GB // 2) as r:
                for odd in range(2):
                    filter_group(r * 2 + odd, odd)
            dve.wait_ge(filter_sums, 1)
            then_wait(nc.vector.tensor_copy(flat(tap_sum[:]), ps_d[:, 0:2 * G]))
            dve.wait_ge(small_loaded, 112)
            with dve.Fori(1, BLOCKS) as k:
                for gl in range(GB):
                    filter_group(k * GB + gl, gl % 2)
                    if gl in after_group:
                        after_group[gl](k - 1)
            for stage in after_group.values():
                stage(BLOCKS - 1)

            dve.wait_ge(dots_folded, 1)
            nc.vector.tensor_copy(dot_c[:], ps_a[:, 0:CT * B].rearrange("p (t b) -> p t b", b=B)
                                  ).then_inc(dots_copied, 1)
            dve.wait_ge(hidden_ready, 1)
            nc.vector.tensor_tensor(hid[:], ps_b[:, 0:HT * B].rearrange("p (o b) -> p o b", b=B),
                                    bc(lb1_sb[:], B), ALU.add).then_inc(hidden_copied, 1)
            dve.wait_ge(logits_ready, 1)
            then_wait(nc.vector.tensor_tensor(logit, ps_c[0:B, :], lb2_sb[:], ALU.add))
            then_wait(nc.vector.reduce_max(neg_max[:], logit, AX.X))
            nc.vector.tensor_scalar(neg_max[:], neg_max[:], -1.0, None, ALU.mult).then_inc(exp_asked, 1)
            dve.wait_ge(exp_done, 1)
            then_wait(nc.vector.reciprocal(exp_sum[:], exp_sum[:]))
            nc.vector.tensor_scalar(prob, prob, exp_sum[:], None, ALU.mult).then_inc(prob_ready, 1)
            dve.wait_ge(prob_turned, 1)
            nc.vector.tensor_copy(prob_c[:], ps_d[:, 0:CT * B].rearrange("p (t b) -> p t b", b=B)
                                  ).then_inc(prob_copied, 1)
            dve.wait_ge(prob_spread, 1)
            then_wait(nc.vector.tensor_tensor(
                tmp[:].rearrange("p (t l) b -> p t l b", l=GB), rstd[:].rearrange("p (t l) b -> p t l b", l=GB),
                ps_a[:, 0:G * B].rearrange("p (l t b) -> p t l b", l=GB, b=B), ALU.mult))
            then_wait(nc.vector.tensor_scalar(scale[:], tmp[:], 1.0, None, ALU.add))
            then_wait(nc.vector.tensor_tensor(
                shift[:].rearrange("p (t l) b -> p t l b", l=GB), mean_rstd[:].rearrange("p (t l) b -> p t l b", l=GB),
                ps_a[:, 0:G * B].rearrange("p (l t b) -> p t l b", l=GB, b=B), ALU.mult))
            then_wait(nc.vector.tensor_scalar(shift[:], shift[:], -1.0, None, ALU.mult))
            nc.vector.sem_inc(coefs_ready, 1)

            def scale_unit(s, g):
                nc.vector.tensor_scalar(xs[:, s, 0, :], xs[:, s, 0, :], scale[:, g, 0:1], shift[:, g, 0:1],
                                        ALU.mult, ALU.add).then_inc(dve_scaled, 1)

            for s in range(S):
                scale_unit(s, G - S // 2 + s // 2)
            with dve.Fori(0, ROUNDS - 1) as r:
                for s in range(S):
                    dve.wait_ge(x_loaded[s], r * 32 + 32 * (ROUNDS + 1))
                    scale_unit(s, r * 2 + s // 2)


def kernel(**inputs):
    import numpy as np
    import concourse.bacc as bacc
    from concourse.bass_utils import run_bass_kernel_spmd

    a = {k.replace("L0_conv_", ""): np.asarray(v) for k, v in inputs.items()}

    def by_partition(w):
        return w.reshape(G, CG, E, -1).transpose(1, 2, 0, 3).reshape(P, G, -1)

    laid = {
        "x": a["x"],
        "w1": by_partition(a["w1"].reshape(C, H)),
        "w2": by_partition(a["w2"].reshape(C, W)),
        **{n: a[n].reshape(G, CG).T for n in ("g1", "b1", "g2", "b2")},
        "w2_rows": a["w2"].reshape(C, W),
        "lw1": a["lw1"].T, "lb1": a["lb1"].reshape(HT, P).T,
        "lw2": a["lw2"].T, "lb2": a["lb2"].reshape(1, C),
    }
    nc = bacc.Bacc("TRN2", target_bir_lowering=False, num_devices=1)
    arrays, args = {}, []
    for name, v in laid.items():
        arrays[f"in_{name}"] = np.ascontiguousarray(v)
        args.append(nc.dram_tensor(f"in_{name}", v.shape, mybir.dt.from_np(v.dtype), kind="ExternalInput").ap())
    out = nc.dram_tensor("out_0", (B, C, H, W), mybir.dt.float32, kind="ExternalOutput").ap()
    conv_preact(nc, *args, out)
    r = run_bass_kernel_spmd(nc, [arrays], core_ids=[0])
    return r.results[0]["out_0"]
```
